# Optimizing a Trainium2 kernel written in Bass

```python
import numpy as np
import jax
import jax.numpy as jnp

def _softmax(x, axis=-1):
    return jax.nn.softmax(x, axis=axis)

def _gelu(x):
    return jax.nn.gelu(x, approximate=True)

def _silu(x):
    return jax.nn.silu(x)

def _sigmoid(x):
    return jax.nn.sigmoid(x)

def _layernorm(x, axis=-1, eps=1e-05):
    m = jnp.mean(x, axis=axis, keepdims=True)
    v = jnp.var(x, axis=axis, keepdims=True)
    return (x - m) / jnp.sqrt(v + eps)

def _scatter_add(tgt, idx, src, axis=0):
    return tgt.at[idx].add(src)

def _segment_sum(src, seg, n):
    return jax.ops.segment_sum(src, seg, n)
kernel_name = 'mk_dlrm_tower_d1_rec_r8_c69874'

def setup_inputs(seed: int=0):
    np.random.seed(seed)
    _w = jnp.asarray

    def _rec_inputs():
        import jax
        import jax.numpy as jnp
        _tk = jax.random.key(seed)
        dense_ctx = jax.random.normal(jax.random.fold_in(_tk, 190), (512, 16), jnp.float32)
        ids = jnp.stack([jax.random.randint(jax.random.fold_in(_tk, 200 + f), (512,), 0, v, jnp.int32) for f, v in enumerate([12500, 12500, 1250, 1250, 12500, 12500, 1000, 125000, 1000, 1000, 1250, 12500, 12500, 1000, 1000, 1000, 1000, 1250, 1000, 1000, 1000, 1250, 1000, 1250, 12500, 12500, 1250])], axis=1)
        tbl_0 = 0.05 * jax.random.normal(jax.random.fold_in(_tk, 500 + 0), (12500, 128), jnp.float32)
        tbl_1 = 0.05 * jax.random.normal(jax.random.fold_in(_tk, 500 + 1), (12500, 128), jnp.float32)
        tbl_2 = 0.05 * jax.random.normal(jax.random.fold_in(_tk, 500 + 2), (1250, 128), jnp.float32)
        tbl_3 = 0.05 * jax.random.normal(jax.random.fold_in(_tk, 500 + 3), (1250, 128), jnp.float32)
        tbl_4 = 0.05 * jax.random.normal(jax.random.fold_in(_tk, 500 + 4), (12500, 128), jnp.float32)
        tbl_5 = 0.05 * jax.random.normal(jax.random.fold_in(_tk, 500 + 5), (12500, 128), jnp.float32)
        tbl_6 = 0.05 * jax.random.normal(jax.random.fold_in(_tk, 500 + 6), (1000, 128), jnp.float32)
        tbl_7 = 0.05 * jax.random.normal(jax.random.fold_in(_tk, 500 + 7), (125000, 128), jnp.float32)
        tbl_8 = 0.05 * jax.random.normal(jax.random.fold_in(_tk, 500 + 8), (1000, 128), jnp.float32)
        tbl_9 = 0.05 * jax.random.normal(jax.random.fold_in(_tk, 500 + 9), (1000, 128), jnp.float32)
        tbl_10 = 0.05 * jax.random.normal(jax.random.fold_in(_tk, 500 + 10), (1250, 128), jnp.float32)
        tbl_11 = 0.05 * jax.random.normal(jax.random.fold_in(_tk, 500 + 11), (12500, 128), jnp.float32)
        tbl_12 = 0.05 * jax.random.normal(jax.random.fold_in(_tk, 500 + 12), (12500, 128), jnp.float32)
        tbl_13 = 0.05 * jax.random.normal(jax.random.fold_in(_tk, 500 + 13), (1000, 128), jnp.float32)
        tbl_14 = 0.05 * jax.random.normal(jax.random.fold_in(_tk, 500 + 14), (1000, 128), jnp.float32)
        tbl_15 = 0.05 * jax.random.normal(jax.random.fold_in(_tk, 500 + 15), (1000, 128), jnp.float32)
        tbl_16 = 0.05 * jax.random.normal(jax.random.fold_in(_tk, 500 + 16), (1000, 128), jnp.float32)
        tbl_17 = 0.05 * jax.random.normal(jax.random.fold_in(_tk, 500 + 17), (1250, 128), jnp.float32)
        tbl_18 = 0.05 * jax.random.normal(jax.random.fold_in(_tk, 500 + 18), (1000, 128), jnp.float32)
        tbl_19 = 0.05 * jax.random.normal(jax.random.fold_in(_tk, 500 + 19), (1000, 128), jnp.float32)
        tbl_20 = 0.05 * jax.random.normal(jax.random.fold_in(_tk, 500 + 20), (1000, 128), jnp.float32)
        tbl_21 = 0.05 * jax.random.normal(jax.random.fold_in(_tk, 500 + 21), (1250, 128), jnp.float32)
        tbl_22 = 0.05 * jax.random.normal(jax.random.fold_in(_tk, 500 + 22), (1000, 128), jnp.float32)
        tbl_23 = 0.05 * jax.random.normal(jax.random.fold_in(_tk, 500 + 23), (1250, 128), jnp.float32)
        tbl_24 = 0.05 * jax.random.normal(jax.random.fold_in(_tk, 500 + 24), (12500, 128), jnp.float32)
        tbl_25 = 0.05 * jax.random.normal(jax.random.fold_in(_tk, 500 + 25), (12500, 128), jnp.float32)
        tbl_26 = 0.05 * jax.random.normal(jax.random.fold_in(_tk, 500 + 26), (1250, 128), jnp.float32)
        _rk = jax.random.fold_in(_tk, 7)
        W_top1 = 0.0521996 * jax.random.normal(jax.random.fold_in(_tk, 801), (367, 512), jnp.float32)
        W_top2 = 0.0441942 * jax.random.normal(jax.random.fold_in(_tk, 802), (512, 256), jnp.float32)
        W_top3 = 0.0625 * jax.random.normal(jax.random.fold_in(_tk, 803), (256, 1), jnp.float32)
        b_top1 = jnp.zeros((512,), jnp.float32)
        b_top2 = jnp.zeros((256,), jnp.float32)
        return (dense_ctx, ids, tbl_0, tbl_1, tbl_2, tbl_3, tbl_4, tbl_5, tbl_6, tbl_7, tbl_8, tbl_9, tbl_10, tbl_11, tbl_12, tbl_13, tbl_14, tbl_15, tbl_16, tbl_17, tbl_18, tbl_19, tbl_20, tbl_21, tbl_22, tbl_23, tbl_24, tbl_25, tbl_26, W_top1, b_top1, W_top2, b_top2, W_top3)
    dense_ctx, ids, tbl_0, tbl_1, tbl_2, tbl_3, tbl_4, tbl_5, tbl_6, tbl_7, tbl_8, tbl_9, tbl_10, tbl_11, tbl_12, tbl_13, tbl_14, tbl_15, tbl_16, tbl_17, tbl_18, tbl_19, tbl_20, tbl_21, tbl_22, tbl_23, tbl_24, tbl_25, tbl_26, W_top1, b_top1, W_top2, b_top2, W_top3 = _rec_inputs()

    def _L0_rec_setup():
        import jax, jax.numpy as jnp
        import numpy as np
        key = jax.random.key(seed)
        B, F, D = (2048, 27, 128)
        inputs = jax.random.normal(key, (B, F, D), dtype=jnp.float32)
        return {'inputs': inputs, 'num_feas': F}
    _L0_rec_all = _L0_rec_setup()
    _L0_rec_in = {k: v for k, v in _L0_rec_all.items() if k in ()}
    del _L0_rec_all
    return {'dense_ctx': dense_ctx, 'ids': ids, 'tbl_0': tbl_0, 'tbl_1': tbl_1, 'tbl_2': tbl_2, 'tbl_3': tbl_3, 'tbl_4': tbl_4, 'tbl_5': tbl_5, 'tbl_6': tbl_6, 'tbl_7': tbl_7, 'tbl_8': tbl_8, 'tbl_9': tbl_9, 'tbl_10': tbl_10, 'tbl_11': tbl_11, 'tbl_12': tbl_12, 'tbl_13': tbl_13, 'tbl_14': tbl_14, 'tbl_15': tbl_15, 'tbl_16': tbl_16, 'tbl_17': tbl_17, 'tbl_18': tbl_18, 'tbl_19': tbl_19, 'tbl_20': tbl_20, 'tbl_21': tbl_21, 'tbl_22': tbl_22, 'tbl_23': tbl_23, 'tbl_24': tbl_24, 'tbl_25': tbl_25, 'tbl_26': tbl_26, 'W_top1': W_top1, 'b_top1': b_top1, 'W_top2': W_top2, 'b_top2': b_top2, 'W_top3': W_top3}

def reference(dense_ctx, ids, tbl_0, tbl_1, tbl_2, tbl_3, tbl_4, tbl_5, tbl_6, tbl_7, tbl_8, tbl_9, tbl_10, tbl_11, tbl_12, tbl_13, tbl_14, tbl_15, tbl_16, tbl_17, tbl_18, tbl_19, tbl_20, tbl_21, tbl_22, tbl_23, tbl_24, tbl_25, tbl_26, W_top1, b_top1, W_top2, b_top2, W_top3):
    import jax
    import jax.numpy as jnp

    def _L0_rec_ref(inputs, num_feas):
        import jax, jax.numpy as jnp
        import numpy as np
        dot_products = jnp.einsum('bnd,bmd->bnm', inputs, inputs)
        r, c = np.tril_indices(num_feas, k=-1)
        flat_interactions = dot_products[:, c, r]
        return flat_interactions
    e = jnp.stack([tbl_0[ids[:, 0]], tbl_1[ids[:, 1]], tbl_2[ids[:, 2]], tbl_3[ids[:, 3]], tbl_4[ids[:, 4]], tbl_5[ids[:, 5]], tbl_6[ids[:, 6]], tbl_7[ids[:, 7]], tbl_8[ids[:, 8]], tbl_9[ids[:, 9]], tbl_10[ids[:, 10]], tbl_11[ids[:, 11]], tbl_12[ids[:, 12]], tbl_13[ids[:, 13]], tbl_14[ids[:, 14]], tbl_15[ids[:, 15]], tbl_16[ids[:, 16]], tbl_17[ids[:, 17]], tbl_18[ids[:, 18]], tbl_19[ids[:, 19]], tbl_20[ids[:, 20]], tbl_21[ids[:, 21]], tbl_22[ids[:, 22]], tbl_23[ids[:, 23]], tbl_24[ids[:, 24]], tbl_25[ids[:, 25]], tbl_26[ids[:, 26]]], axis=1)
    z = _L0_rec_ref(e, 27)
    z = z.reshape(z.shape[0], -1)
    h = jnp.concatenate([z, dense_ctx], axis=1)
    h = jnp.maximum(h @ W_top1 + b_top1, 0.0)
    h = jnp.maximum(h @ W_top2 + b_top2, 0.0)
    y = h @ W_top3
    return y

_drawn_inputs = setup_inputs


def setup_inputs(seed=0):
    import zlib

    import numpy as np

    out = dict(_drawn_inputs(seed))
    spreads = {'b_top1': (0.0, 0.1), 'b_top2': (0.0, 0.1)}
    factors = {}
    for name, (base, spread) in spreads.items():
        noise = np.random.default_rng([zlib.crc32(name.encode()), seed]).standard_normal(out[name].shape)
        drawn = base * np.exp(spread * noise) if base else spread * noise
        out[name] = jnp.asarray(drawn.astype(out[name].dtype))
    for name, factor in factors.items():
        out[name] = (out[name] * factor).astype(out[name].dtype)
    return out
```

```python
import concourse.bass as bass
from concourse import mybir
from contextlib import ExitStack

F32 = mybir.dt.float32
I32 = mybir.dt.int32
U32 = mybir.dt.uint32
ALU = mybir.AluOpType
ACT = mybir.ActivationFunctionType


def build_tower(nc, dense_ctx, ids, tables, W_top1, b_top1, W_top2, b_top2, W_top3, out):
    P = 128
    B, NF = ids.shape
    D = tables[0].shape[1]
    ND = dense_ctx.shape[1]
    NPAIR = NF * (NF - 1) // 2
    NZ, H1 = W_top1.shape
    H2 = W_top2.shape[1]
    assert D == P and B % P == 0 and NZ == NPAIR + ND and NF <= 32
    NT = B // P
    SLOTS = 2
    FP = 32
    SG = P // FP
    NG = P // SG
    TPB = 512 // P
    FGROUPS = [(f, min(TPB, NF - f)) for f in range(0, NF, TPB)]
    MGROUPS = [(m, min(TPB, NF - m)) for m in range(1, NF, TPB)]
    NFG, NMG = len(FGROUPS), len(MGROUPS)
    GPB = TPB
    NGB = NG // GPB
    KZ = [(k, min(P, NZ - k)) for k in range(0, NZ, P)]
    C1, C2 = H1 // P, H2 // P
    NB_ROWS = 2 * C2 + C1
    HC1 = C1 // 2
    assert HC1 == 2 and C2 == 2 and NT % SLOTS == 0 and NGB % 2 == 0

    with ExitStack() as ctx:
        def sb(name, shape, dt=F32):
            return ctx.enter_context(nc.sbuf_tensor(name, shape, dt))

        def psum(name, shape):
            return ctx.enter_context(nc.psum_tensor(name, shape, F32))

        def sem(name):
            return ctx.enter_context(nc.semaphore(name))

        idx = sb("idx", [P, NT, NF], I32)
        rows = sb("rows", [P, SLOTS, NF, D])
        cols = sb("cols", [P, SLOTS, P, FP])
        gram = sb("gram", [P, SLOTS, NF, NG])
        z = sb("z", [NG, SLOTS, SG, NZ])
        zT = sb("zT", [P, len(KZ), P])
        h1T = sb("h1T", [P, C1, P])
        h2T = sb("h2T", [P, C2, P])
        y = sb("y", [1, NT, NG, SG])
        w1 = sb("w1", [P, len(KZ), H1])
        w2 = sb("w2", [P, C1, H2])
        small_rows = sb("small_rows", [NB_ROWS, P])
        small = sb("small", [P, NB_ROWS])
        ident = sb("ident", [P, P])

        ps_cols = [psum(f"ps_cols{i}", [P, TPB, P]) for i in range(2)]
        ps_gram = [psum(f"ps_gram{i}", [P, GPB, P]) for i in range(2)]
        ps_pick = [psum(f"ps_pick{i}", [P, TPB, P]) for i in range(2)]
        ps_z = psum("ps_z", [P, 4, P])
        ps_h = psum("ps_h", [P, 4, P])
        bank_of = [ps_h, ps_z]

        ids_in = sem("ids_in")
        w1_in = sem("w1_in")
        w2_in = sem("w2_in")
        small_in = sem("small_in")
        dense_in = [sem(f"dense_in{s}") for s in range(SLOTS)]
        ident_zero = sem("ident_zero")
        ident_ready = sem("ident_ready")
        pad_ready = sem("pad_ready")
        rows_in = [[sem(f"rows_in{s}_{k}") for k in range(NFG)] for s in range(SLOTS)]
        small_turned = sem("small_turned")
        small_ready = sem("small_ready")
        rows_turned = sem("rows_turned")
        cols_ready = [sem("cols_ready_dve"), sem("cols_ready_act")]
        gram_made = sem("gram_made")
        gram_ready = [sem("gram_ready_dve"), sem("gram_ready_act")]
        gram_turned = sem("gram_turned")
        z_ready = [sem("z_ready_dve"), sem("z_ready_act")]
        z_turned = sem("z_turned")
        zT_ready = sem("zT_ready")
        h1_made = sem("h1_made")
        h1_ready = [sem("h1_ready_dve"), sem("h1_ready_act")]
        h2_made = sem("h2_made")
        h2_ready = [sem("h2_ready_dve"), sem("h2_ready_act")]
        y_made = sem("y_made")
        y_ready = sem("y_ready")
        out_done = sem("out_done")

        w3_col = C1 + C2
        block = ctx.enter_context(nc.Block())

        @block.sync
        def _(sp):
            sp.dma_start(idx[:], ids.rearrange("(t p) f -> p t f", p=P)).then_inc(ids_in, 16)
            sp.dma_start(small_rows[0:C1, :], b_top1.rearrange("(c p) -> c p", p=P)).then_inc(small_in, 16)
            sp.dma_start(small_rows[C1:C1 + C2, :], b_top2.rearrange("(c p) -> c p", p=P)).then_inc(small_in, 16)
            sp.dma_start(small_rows[w3_col:w3_col + C2, :],
                         W_top3.rearrange("(c p) one -> c (p one)", p=P)).then_inc(small_in, 16)
            nfull = NZ // P
            sp.dma_start(w1[:, 0:nfull, :],
                         W_top1[0:nfull * P, :].rearrange("(k p) o -> p k o", p=P)).then_inc(w1_in, 16)
            sp.dma_start(w1[0:NZ - nfull * P, nfull, :], W_top1[nfull * P:NZ, :]).then_inc(w1_in, 16)
            sp.dma_start(w2[:], W_top2.rearrange("(k p) o -> p k o", p=P)).then_inc(w2_in, 16)
            dense = dense_ctx.rearrange("(t g s) d -> t g s d", t=NT, s=SG)
            for t in range(NT):
                if t >= SLOTS:
                    sp.wait_ge(z_turned, t - SLOTS + 1)
                sp.dma_start(z[:, t % SLOTS, :, NPAIR:NZ], dense[t]).then_inc(dense_in[t % SLOTS], 16)
            sp.wait_ge(y_ready, NT)
            sp.dma_start(out.rearrange("b one -> one b"), y[:].rearrange("p t g s -> p (t g s)")).then_inc(out_done, 16)
            sp.wait_ge(out_done, 16)

        @block.gpsimd
        def _(pool):
            nc.gpsimd.memset(ident[:], 0.0).then_inc(ident_zero, 1)
            pool.wait_ge(ident_zero, 1)
            nc.gpsimd.affine_select(out=ident[:], in_=ident[:], compare_op=ALU.not_equal, fill=1.0, base=0,
                                    pattern=[[-1, P]], channel_multiplier=1).then_inc(ident_ready, 1)
            pool.wait_ge(ids_in, 16)
            for t in range(NT):
                for k, (f0, nf) in enumerate(FGROUPS):
                    if t >= SLOTS:
                        pool.wait_ge(rows_turned, NFG * (t - SLOTS) + k + 1)
                    for f in range(f0, f0 + nf):
                        nc.gpsimd.indirect_dma_start(
                            out=rows[:, t % SLOTS, f, :], out_offset=None, in_=tables[f],
                            in_offset=bass.IndirectOffsetOnAxis(ap=idx[:, t, f:f + 1].bitcast(U32), axis=0),
                        ).then_inc(rows_in[t % SLOTS][k], 16)

        @block.tensor
        def _(pe):
            pe.wait_ge(ident_ready, 1)
            pe.wait_ge(small_in, 48)
            nc.tensor.transpose(ps_z[:, 0, 0:NB_ROWS], small_rows[:, :],
                                ident[0:NB_ROWS, 0:NB_ROWS]).then_inc(small_turned, 1)
            pe.wait_ge(small_ready, 1)
            pe.wait_ge(pad_ready, 1)
            pe.wait_ge(w1_in, 32)
            pe.wait_ge(w2_in, 16)

            for pair in range(NT // SLOTS):
                for slot in range(SLOTS):
                    t = pair * SLOTS + slot
                    for k, (f0, nf) in enumerate(FGROUPS):
                        q = slot * NFG + k
                        pe.wait_ge(rows_in[slot][k], pair * (16 * nf) + 16 * nf)
                        pe.wait_ge(cols_ready[q % 2], pair * NFG + q // 2)
                        for j in range(nf):
                            last = nc.tensor.transpose(ps_cols[q % 2][:, j, :], rows[:, slot, f0 + j, :], ident[:])
                        last.then_inc(rows_turned, 1)
                    for e in range(2):
                        done = [q for q in range((slot + 1) * NFG) if q % 2 == e]
                        pe.wait_ge(cols_ready[e], pair * NFG + len(done))
                    for gb in range(NGB):
                        pe.wait_ge(gram_ready[gb % 2], t * (NGB // 2) + gb // 2)
                        for j in range(GPB):
                            s0 = (gb * GPB + j) * SG
                            group = cols[:, slot, s0:s0 + SG, :]
                            last = nc.tensor.matmul(
                                ps_gram[gb % 2][:, j, 0:SG * NF].rearrange("p (s m) -> p s m", s=SG),
                                group.rearrange("p s f -> p (s f)"), group[:, :, 0:NF], start=True, stop=True)
                        last.then_inc(gram_made, 1)
                    for e in range(2):
                        pe.wait_ge(gram_ready[e], t * (NGB // 2) + NGB // 2)
                    for k, (m0, nm) in enumerate(MGROUPS):
                        q = slot * NMG + k
                        pe.wait_ge(z_ready[q % 2], pair * NMG + q // 2)
                        for j in range(nm):
                            last = nc.tensor.transpose(ps_pick[q % 2][0:NG, j, :], gram[:, slot, m0 + j, :], ident[:])
                        last.then_inc(gram_turned, 1)
                    for e in range(2):
                        done = [q for q in range((slot + 1) * NMG) if q % 2 == e]
                        pe.wait_ge(z_ready[e], pair * NMG + len(done))
                    pe.wait_ge(dense_in[slot], pair * 16 + 16)
                    pe.wait_ge(y_ready, t)
                    for k, (k0, nk) in enumerate(KZ):
                        for s in range(SG):
                            last = nc.tensor.transpose(ps_z[0:nk, k, s * NG:(s + 1) * NG],
                                                       z[:, slot, s, k0:k0 + nk], ident[0:NG, 0:NG])
                    last.then_inc(z_turned, 1)
                    pe.wait_ge(zT_ready, t * 1 + 1)
                    for c in range(C1):
                        for k, (k0, nk) in enumerate(KZ):
                            last = nc.tensor.matmul(bank_of[c // HC1][:, c % HC1, :], w1[0:nk, k, c * P:(c + 1) * P], zT[0:nk, k, :],
                                                    start=(k == 0), stop=(k == len(KZ) - 1))
                        if c % HC1 == HC1 - 1:
                            last.then_inc(h1_made, 1)
                    for e in range(2):
                        pe.wait_ge(h1_ready[e], t + 1)
                    for c in range(C2):
                        for k in range(C1):
                            last = nc.tensor.matmul(bank_of[c][:, HC1, :], w2[:, k, c * P:(c + 1) * P], h1T[:, k, :],
                                                    start=(k == 0), stop=(k == C1 - 1))
                        last.then_inc(h2_made, 1)
                    for e in range(2):
                        pe.wait_ge(h2_ready[e], t + 1)
                    for k in range(C2):
                        last = nc.tensor.matmul(ps_z[0:1, 3, :], small[:, w3_col + k:w3_col + k + 1], h2T[:, k, :],
                                                start=(k == 0), stop=(k == C2 - 1))
                    last.then_inc(y_made, 1)

        def copies(eng, e, copy, relu, pair, slot):
            t = pair * SLOTS + slot
            for k, (f0, nf) in enumerate(FGROUPS):
                q = slot * NFG + k
                if q % 2 == e:
                    eng.wait_ge(rows_turned, pair * (SLOTS * NFG) + q + 1)
                    copy(cols[:, slot, :, f0:f0 + nf].rearrange("p b f -> p f b"),
                         ps_cols[e][:, 0:nf, :]).then_inc(cols_ready[e], 1)
            for gb in range(e, NGB, 2):
                eng.wait_ge(gram_made, t * NGB + gb + 1)
                for s in range(SG):
                    quad = slice(s * FP, (s + 1) * FP)
                    last = copy(gram[quad, slot, :, gb * GPB:(gb + 1) * GPB].rearrange("p m g -> p g m"),
                                ps_gram[e][quad, :, s * NF:(s + 1) * NF])
                last.then_inc(gram_ready[e], 1)
            for k, (m0, nm) in enumerate(MGROUPS):
                q = slot * NMG + k
                if q % 2 == e:
                    eng.wait_ge(gram_turned, pair * (SLOTS * NMG) + q + 1)
                    for j in range(nm):
                        m = m0 + j
                        last = copy(z[:, slot, :, m * (m - 1) // 2:m * (m + 1) // 2],
                                    ps_pick[e][0:NG, j, :].rearrange("p (s n) -> p s n", s=SG)[:, :, 0:m])
                    last.then_inc(z_ready[e], 1)
            if e == 0:
                eng.wait_ge(z_turned, t + 1)
                copy(zT[:, 0:NZ // P, :], ps_z[:, 0:NZ // P, :])
                copy(zT[0:NZ % P, NZ // P, :], ps_z[0:NZ % P, NZ // P, :]).then_inc(zT_ready, 1)
            eng.wait_ge(h1_made, t * 2 + e + 1)
            for j in range(HC1):
                c = e * HC1 + j
                last = relu(h1T[:, c, :], bank_of[e][:, j, :], small[:, c:c + 1])
            last.then_inc(h1_ready[e], 1)
            eng.wait_ge(h2_made, t * 2 + e + 1)
            relu(h2T[:, e, :], bank_of[e][:, HC1, :], small[:, C1 + e:C1 + e + 1]).then_inc(h2_ready[e], 1)

        @block.vector
        def _(dve):
            nc.vector.memset(cols[:, :, :, NF:FP], 0.0).then_inc(pad_ready, 1)
            dve.wait_ge(small_turned, 1)
            nc.vector.tensor_copy(small[:], ps_z[:, 0, 0:NB_ROWS]).then_inc(small_ready, 1)
            dve.wait_ge(small_ready, 1)

            def relu(o, i, bias):
                return nc.vector.tensor_scalar(o, i, bias, 0.0, ALU.add, ALU.max)

            with dve.Fori(0, NT // SLOTS) as pair:
                for slot in range(SLOTS):
                    copies(dve, 0, nc.vector.tensor_copy, relu, pair, slot)

        @block.scalar
        def _(act):
            act.wait_ge(small_ready, 1)

            def relu(o, i, bias):
                return nc.scalar.activation(o, i, ACT.Relu, bias=bias)

            with act.Fori(0, NT // SLOTS) as pair:
                for slot in range(SLOTS):
                    t = pair * SLOTS + slot
                    copies(act, 1, nc.scalar.copy, relu, pair, slot)
                    act.wait_ge(y_made, t + 1)
                    nc.scalar.copy(y[:, bass.ds(t, 1), :, :].rearrange("p t g s -> p (t s) g"),
                                   ps_z[0:1, 3, :].rearrange("p (s g) -> p s g", s=SG)).then_inc(y_ready, 1)


N_TABLES = 27
INPUTS = (["dense_ctx", "ids"] + [f"tbl_{i}" for i in range(N_TABLES)]
          + ["W_top1", "b_top1", "W_top2", "b_top2", "W_top3"])


def kernel(**inputs):
    import numpy as np
    import concourse.bacc as bacc
    from concourse.bass_utils import run_bass_kernel_spmd

    nc = bacc.Bacc("TRN2", target_bir_lowering=False, num_devices=1)
    arrays, args = {}, {}
    for name in INPUTS:
        a = np.ascontiguousarray(inputs[name])
        arrays[f"in_{name}"] = a
        args[name] = nc.dram_tensor(f"in_{name}", a.shape, mybir.dt.from_np(a.dtype), kind="ExternalInput").ap()
    out = nc.dram_tensor("out_y", (arrays["in_ids"].shape[0], 1), F32, kind="ExternalOutput").ap()
    build_tower(nc, args["dense_ctx"], args["ids"], [args[f"tbl_{i}"] for i in range(N_TABLES)],
                args["W_top1"], args["b_top1"], args["W_top2"], args["b_top2"], args["W_top3"], out)
    r = run_bass_kernel_spmd(nc, [arrays], core_ids=[0])
    return r.results[0]["out_y"]
```

```python
import concourse.bass as bass
from concourse import mybir
from contextlib import ExitStack

F32 = mybir.dt.float32
F16 = mybir.dt.float16
BF16 = mybir.dt.bfloat16
I32 = mybir.dt.int32
U32 = mybir.dt.uint32
ALU = mybir.AluOpType
ACT = mybir.ActivationFunctionType


def arithmetic_runs(features, longest):
    runs, i = [], 0
    while i < len(features):
        n, step = 1, 1
        if i + 1 < len(features):
            step = features[i + 1] - features[i]
            while n < longest and i + n < len(features) and features[i + n] - features[i + n - 1] == step:
                n += 1
        runs.append((features[i], step, n))
        i += n
    return runs


def build_tower(nc, dense_ctx, ids, tables, W_top1, b_top1, W_top2, b_top2, W_top3, out):
    P = 128
    B, NF = ids.shape
    D = tables[0].shape[1]
    ND = dense_ctx.shape[1]
    NPAIR = NF * (NF - 1) // 2
    NZ, H1 = W_top1.shape
    H2 = W_top2.shape[1]
    NT = B // P
    PAIR = 2
    NPR = NT // PAIR
    SLOTS = PAIR
    FP = 32
    SG = P // FP
    NG = P // SG
    ROWS = (SG - 1) * FP + NF - 1
    TPB = 512 // P
    KZ = [(k, min(P, NZ - k)) for k in range(0, NZ, P)]
    LASTK = len(KZ) - 1
    C1, C2 = H1 // P, H2 // P
    HC1 = C1 // 2
    NB_ROWS = 2 * C2 + C1
    w3_col = C1 + C2
    assert D == P and B == NT * P and NT % PAIR == 0 and NZ == NPAIR + ND and NF <= FP
    assert HC1 == 2 and C2 == 2

    ONE_HOT = [13, 14, 15, 16, 18, 19, 20]
    HOTS = [4, 7]
    TP = 125
    RPP = [tables[f].shape[0] // TP for f in ONE_HOT]
    assert all(tables[f].shape[0] == TP * r for f, r in zip(ONE_HOT, RPP))
    assert all(tables[f].shape[0] <= 2048 for f in ONE_HOT)
    MAXR = max(RPP)
    GATHERED = [[f for f in range(NF) if f not in ONE_HOT[:n]] for n in HOTS]
    PLACE = {f: i for i, f in enumerate(GATHERED[0])}
    RUNS = [arithmetic_runs(g, TPB) for g in GATHERED]
    assert set(GATHERED[1]) <= set(GATHERED[0])
    GPB = 512 // (SG * (NF - 1))
    NGB = NG // GPB

    PICKS = [range(0, 4), range(4, -(-(NF - 1) // TPB))]
    CHUNKS = [[range(0, 1)], [range(1, LASTK), range(LASTK, LASTK + 1)]]
    assert NPAIR > KZ[0][1] and (PICKS[0][-1] + 1) * TPB * ((PICKS[0][-1] + 1) * TPB + 1) // 2 >= KZ[0][1]
    CHAIN = [("products", None), ("pick", 0), ("pick", 1), ("pairs", 0), ("pairs", 1), ("layer1", 0), ("layer1", 1),
             ("layer2", None), ("layer3", None)]
    LAST_CHAIN = [("products", None), ("warm", 12), ("pick", 0), ("warm", 6), ("pairs", 0), ("warm", 6), ("pick", 1),
                  ("layer1", 0), ("warm", 4), ("pairs", 1), ("warm", 8), ("layer1", 1), ("layer2", None), ("layer3", None)]
    GAPS = [("products", None), ("pick", 0), ("pick", 1), ("pairs", 1), ("layer1", 1), ("layer2", None), ("layer3", None)]

    def chain(t, between):
        stages = []
        for kind, what in CHAIN:
            stages.append((kind, t, what))
            if (kind, what) in GAPS:
                stages += between.get(GAPS.index((kind, what)), [])
        return stages

    def hot(pair, *which):
        return [("one_hot", pair, i) for i in which]

    def turns(t, *which):
        return [("turn", t, k) for k in which]

    def warm(n):
        return [("warm", None, n)]

    def split(*which):
        return [("split", None, i) for i in which]

    assert NPR == 2 and NT == 4
    ORDER = split(0) + hot(0, 0) + split(1) + hot(1, 0) + turns(0, 0) + hot(0, 1) + split(2) + hot(1, 1) + turns(0, 1) + hot(0, 2)
    ORDER += split(3) + turns(0, 2) + hot(1, 2) + turns(0, 3) + hot(0, 3) + split(4) + turns(0, 4, 5, 6)
    ORDER += hot(1, 3) + chain(0, {0: turns(1, 0), 1: turns(1, 1), 2: turns(1, 2), 3: turns(1, 3), 4: hot(1, 4), 5: turns(1, 4), 6: turns(1, 5)})
    ORDER += split(5, 6) + turns(1, 6) + hot(1, 5)
    ORDER += chain(1, {0: turns(2, 0), 1: turns(2, 1), 2: turns(2, 2), 3: turns(2, 3), 4: hot(1, 6), 5: turns(2, 4, 5)})
    ORDER += chain(2, {0: turns(3, 0), 1: turns(3, 1), 2: turns(3, 2), 3: turns(3, 3), 5: turns(3, 4, 5)})
    ORDER += [(kind, NT - 1, what) for kind, what in LAST_CHAIN]
    counted = [stage for stage in ORDER if stage[0] != "warm"]
    assert len(set(counted)) == len(counted)
    assert len(counted) == sum(PAIR * (len(r) + len(CHAIN)) for r in RUNS) + sum(HOTS) + len(ONE_HOT)

    WORK = 3
    uses = {("products", None): NGB, ("pick", 0): len(PICKS[0]), ("pick", 1): len(PICKS[1]), ("pairs", 0): 1,
            ("pairs", 1): 2, ("layer1", 0): 0, ("layer1", 1): 2, ("layer2", None): 2, ("layer3", None): 1}
    turn_no, hot_no, work_no = {}, {}, {}
    n_work = 0
    for kind, t, what in ORDER:
        if kind == "turn":
            turn_no[t, what] = len(turn_no)
        elif kind == "one_hot":
            hot_no[t, what] = len(hot_no)
        elif kind not in ("split", "warm"):
            work_no[kind, t, what] = n_work
            n_work += uses[kind, what]
    hot_stage = {n: stage for stage, n in hot_no.items()}
    first_use = [min(s for s in hot_no if s[1] == i) for i in range(len(ONE_HOT))]
    assert [hot_no[s] for s in first_use] == sorted(hot_no[s] for s in first_use)

    def work_end(kind, t, what=None):
        return work_no[kind, t, what] + uses[kind, what]

    def uses_of(e, n):
        return (n + 1 - e) // 2

    def hots_before(n):
        return sum(RPP[hot_stage[m][1]] for m in range(n))

    with ExitStack() as ctx:
        def sb(name, shape, dt=F32):
            return ctx.enter_context(nc.sbuf_tensor(name, shape, dt))

        def psum(name, shape, dt=F32):
            return ctx.enter_context(nc.psum_tensor(name, shape, dt))

        def layer1_bank(t, u):
            return ps_hot[u % 2] if t == NT - 1 else ps_work[u % WORK]

        def upper_half(x):
            return x.bitcast(BF16)[:, :, 1::2]

        def sem(name):
            return ctx.enter_context(nc.semaphore(name))

        idx = sb("idx", [P, NT, NF], I32)
        rows = sb("rows", [P, SLOTS, len(PLACE), D])
        cols = sb("cols", [P, NT, P, FP])
        gram = sb("gram", [ROWS, NF, NG])
        z = sb("z", [NG, SLOTS, SG, NZ])
        zT = sb("zT", [P, len(KZ), P])
        h1T = sb("h1T", [P, C1, P])
        h2T = sb("h2T", [P, C2, P])
        y = sb("y", [1, NT, NG, SG])
        w1 = sb("w1", [P, len(KZ), H1])
        w2 = sb("w2", [P, C1, H2])
        small_rows = sb("small_rows", [NB_ROWS, P])
        small = sb("small", [P, NB_ROWS])
        ident = sb("ident", [P, P])
        table = [sb(f"table{i}", [TP, RPP[i], D]) for i in range(len(ONE_HOT))]
        left = [sb(f"left{i}", [TP, RPP[i], D]) for i in range(len(ONE_HOT))]
        low = [sb(f"low{i}", [TP, RPP[i], D], BF16) for i in range(len(ONE_HOT))]
        row_no_int = sb("row_no_int", [P, 2, MAXR], I32)
        row_no = {r: sb(f"row_no{r}", [P, r]) for r in sorted(set(RPP))}
        wide_ids = sb("wide_ids", [P, 2, PAIR, P], F16)
        hot_ids = sb("hot_ids", [P, len(hot_no), PAIR * P], F16)
        one_hot = sb("one_hot", [TP, 2, MAXR, PAIR * P], BF16)
        ident16 = sb("ident16", [P, P], F16)

        ps_cols = [psum(f"ps_cols{i}", [P, TPB, P]) for i in range(2)]
        ps_work = [psum(f"ps_work{i}", [P, TPB, P]) for i in range(WORK)]
        ps_ids = psum("ps_ids", [P, PAIR, P], F16)
        ps_hot = [psum(f"ps_hot{i}", [P, PAIR, P]) for i in range(2)]

        ids_in = sem("ids_in")
        w1_in = sem("w1_in")
        w2_in = sem("w2_in")
        small_in = sem("small_in")
        table_in = [sem(f"table_in{i}") for i in range(len(ONE_HOT))]
        dense_in = [sem(f"dense_in{s}") for s in range(SLOTS)]
        ident_zero = sem("ident_zero")
        ident_ready = sem("ident_ready")
        ident16_ready = sem("ident16_ready")
        left_ready = sem("left_ready")
        low_ready = sem("low_ready")
        row_no_made = sem("row_no_made")
        row_no_ready = sem("row_no_ready")
        pad_ready = sem("pad_ready")
        rows_in = [[sem(f"rows_in{s}_{k}") for k in range(max(map(len, RUNS)))] for s in range(SLOTS)]
        small_turned = sem("small_turned")
        small_ready = sem("small_ready")
        wide_ready = sem("wide_ready")
        ids_turned = sem("ids_turned")
        hot_ids_ready = sem("hot_ids_ready")
        hot_ready = sem("hot_ready")
        hot_made = sem("hot_made")
        hot_cols = sem("hot_cols")
        rows_turned = sem("rows_turned")
        cols_ready = sem("cols_ready")
        work_made = sem("work_made")
        work_out = [sem("work_out_dve"), sem("work_out_act")]
        out_done = sem("out_done")

        block = ctx.enter_context(nc.Block())

        @block.sync
        def _(sp):
            sp.dma_start(idx[:], ids.rearrange("(t p) f -> p t f", p=P)).then_inc(ids_in, 16)
            wide = TP // 16 * 16
            for i, f in enumerate(ONE_HOT):
                whole = tables[f].rearrange("(p r) d -> p r d", p=TP)
                sp.dma_start(table[i][0:wide], whole[0:wide]).then_inc(table_in[i], 16)
                sp.dma_start(table[i][wide:TP], whole[wide:TP]).then_inc(table_in[i], 16)
                if i == 0:
                    sp.dma_start(small_rows[0:C1, :], b_top1.rearrange("(c p) -> c p", p=P)).then_inc(small_in, 16)
                    sp.dma_start(small_rows[C1:C1 + C2, :],
                                 b_top2.rearrange("(c p) -> c p", p=P)).then_inc(small_in, 16)
                    sp.dma_start(small_rows[w3_col:w3_col + C2, :],
                                 W_top3.rearrange("(c p) one -> c (p one)", p=P)).then_inc(small_in, 16)
            nfull = NZ // P
            sp.dma_start(w1[:, 0:nfull, :],
                         W_top1[0:nfull * P, :].rearrange("(k p) o -> p k o", p=P)).then_inc(w1_in, 16)
            sp.dma_start(w1[0:NZ - nfull * P, nfull, :], W_top1[nfull * P:NZ, :]).then_inc(w1_in, 16)
            sp.dma_start(w2[:], W_top2.rearrange("(k p) o -> p k o", p=P)).then_inc(w2_in, 16)
            dense = dense_ctx.rearrange("(t g s) d -> t g s d", t=NT, s=SG)
            for t in range(NT):
                if t >= SLOTS:
                    sp.wait_ge(work_made, work_end("pairs", t - SLOTS, 1))
                sp.dma_start(z[:, t % SLOTS, :, NPAIR:NZ], dense[t]).then_inc(dense_in[t % SLOTS], 16)
            for e in range(2):
                sp.wait_ge(work_out[e], uses_of(e, n_work))
            sp.dma_start(out.rearrange("b one -> one b"),
                         y[:].rearrange("p t g s -> p (t g s)")).then_inc(out_done, 16)
            sp.wait_ge(out_done, 16)

        @block.gpsimd
        def _(pool):
            nc.gpsimd.memset(ident[:], 0.0).then_inc(ident_zero, 1)
            for n, r in enumerate(row_no):
                nc.gpsimd.iota(row_no_int[:, n, 0:r], pattern=[[1, r]], base=0,
                               channel_multiplier=r).then_inc(row_no_made, 1)
            pool.wait_ge(ident_zero, 1)
            nc.gpsimd.affine_select(out=ident[:], in_=ident[:], compare_op=ALU.not_equal, fill=1.0, base=0,
                                    pattern=[[-1, P]], channel_multiplier=1).then_inc(ident_ready, 1)
            pool.wait_ge(ids_in, 16)
            for t in range(NT):
                for k, (f0, step, n) in enumerate(RUNS[t // PAIR]):
                    if t >= SLOTS:
                        last_f = f0 + step * (n - 1)
                        there = [j for j, r in enumerate(RUNS[t // PAIR - 1]) if r[0] <= last_f][-1]
                        pool.wait_ge(rows_turned, turn_no[t - SLOTS, there] + 1)
                    for f in range(f0, f0 + step * n, step):
                        nc.gpsimd.indirect_dma_start(
                            out=rows[:, t % SLOTS, PLACE[f], :], out_offset=None, in_=tables[f],
                            in_offset=bass.IndirectOffsetOnAxis(ap=idx[:, t, f:f + 1].bitcast(U32), axis=0),
                        ).then_inc(rows_in[t % SLOTS][k], 16)

        @block.tensor
        def _(pe):
            def bank_free(u):
                if u >= WORK:
                    pe.wait_ge(work_out[(u - WORK) % 2], uses_of((u - WORK) % 2, u - WORK + 1))

            def copied_out(kind, t, what=None):
                for e in range(2):
                    pe.wait_ge(work_out[e], uses_of(e, work_end(kind, t, what)))

            def spread_ids(n):
                pe.wait_ge(wide_ready, n + 1)
                if n:
                    pe.wait_ge(hot_ids_ready, n)
                for b in range(PAIR):
                    last = nc.tensor.transpose(ps_ids[:, b, :], wide_ids[:, n % 2, b, :], ident16[:])
                last.then_inc(ids_turned, 1)

            def one_hot_products(pair, i):
                n = hot_no[pair, i]
                if n + 2 < len(hot_no):
                    spread_ids(n + 2)
                if n >= 2:
                    pe.wait_ge(hot_cols, n - 1)
                if (pair, i) in first_use:
                    pe.wait_ge(low_ready, i + 1)
                for j in range(RPP[i]):
                    pe.wait_ge(hot_ready, hots_before(n) + j + 1)
                    parts = [upper_half(table[i][:]), upper_half(left[i][:]), low[i]]
                    for q, part in enumerate(parts):
                        last = nc.tensor.matmul(ps_hot[n % 2][:].rearrange("p b s -> p (b s)"),
                                                part[:, j, :], one_hot[:, n % 2, j, :],
                                                start=(j == 0 and q == 0),
                                                stop=(j == RPP[i] - 1 and q == len(parts) - 1))
                last.then_inc(hot_made, 1)

            def turn(t, k):
                f0, step, n = RUNS[t // PAIR][k]
                u = turn_no[t, k]
                before = sum(RUNS[q][k][2] for q in range(t // SLOTS))
                pe.wait_ge(rows_in[t % SLOTS][k], 16 * (before + n))
                if u >= 2:
                    pe.wait_ge(cols_ready, u - 1)
                for j in range(n):
                    last = nc.tensor.transpose(ps_cols[u % 2][:, j, :], rows[:, t % SLOTS, PLACE[f0 + step * j], :], ident[:])
                last.then_inc(rows_turned, 1)

            def products(t, _):
                if t == 0:
                    pe.wait_ge(pad_ready, NT)
                pe.wait_ge(cols_ready, turn_no[t, len(RUNS[t // PAIR]) - 1] + 1)
                pe.wait_ge(hot_cols, max(n for (pair, _), n in hot_no.items() if pair == t // PAIR) + 1)
                width = SG * (NF - 1)
                for gb in range(NGB):
                    u = work_no["products", t, None] + gb
                    bank_free(u)
                    flat = ps_work[u % WORK][:].rearrange("p a b -> p (a b)")
                    for j in range(GPB):
                        s0 = (gb * GPB + j) * SG
                        group = cols[:, t, s0:s0 + SG, :]
                        last = nc.tensor.matmul(
                            flat[0:ROWS, j * width:(j + 1) * width].rearrange("p (s m) -> p s m", s=SG),
                            group.rearrange("p s f -> p (s f)")[:, 0:ROWS], group[:, :, 1:NF], start=True, stop=True)
                    last.then_inc(work_made, 1)

            def pick(t, half):
                if half == 0:
                    copied_out("products", t)
                for b in PICKS[half]:
                    u = work_no["pick", t, half] + b - PICKS[half][0]
                    bank_free(u)
                    m = 1 + b * TPB
                    n = min(TPB, NF - m)
                    nc.tensor.transpose(ps_work[u % WORK][0:n * NG, 0, 0:ROWS],
                                        gram[0:ROWS, m:m + n, :].rearrange("p m g -> p (m g)"),
                                        ident[0:ROWS, 0:ROWS]).then_inc(work_made, 1)

            def pairs(t, half):
                copied_out("pick", t, half)
                for b, chunks in enumerate(CHUNKS[half]):
                    u = work_no["pairs", t, half] + b
                    bank_free(u)
                    if chunks[-1] == LASTK:
                        pe.wait_ge(dense_in[t % SLOTS], 16 * (t // SLOTS + 1))
                    for k in chunks:
                        k0, nk = KZ[k]
                        for s in range(SG):
                            last = nc.tensor.transpose(ps_work[u % WORK][0:nk, k, s * NG:(s + 1) * NG],
                                                       z[:, t % SLOTS, s, k0:k0 + nk], ident[0:NG, 0:NG])
                    last.then_inc(work_made, 1)

            def layer1(t, half):
                copied_out("pairs", t, half)
                if t == 0 and half == 0:
                    pe.wait_ge(w1_in, 32)
                for c in range(C1):
                    u = work_no["layer1", t, 1] + c // HC1
                    if half == 0 and c % HC1 == 0 and t < NT - 1:
                        bank_free(u)
                    for k in [k for chunks in CHUNKS[half] for k in chunks]:
                        nk = KZ[k][1]
                        last = nc.tensor.matmul(layer1_bank(t, u)[:, c % HC1, :], w1[0:nk, k, c * P:(c + 1) * P],
                                                zT[0:nk, k, :], start=(k == 0 and c % HC1 == 0), stop=(k == LASTK),
                                                skip_group_check=True)
                    if half == 1 and c % HC1 == HC1 - 1:
                        last.then_inc(work_made, 1)

            def layer2(t, _):
                if t == 0:
                    pe.wait_ge(w2_in, 16)
                u = work_no["layer2", t, None]
                for half in range(C1 // HC1):
                    made = work_no["layer1", t, 1] + half
                    pe.wait_ge(work_out[made % 2], uses_of(made % 2, made + 1))
                    for c in range(C2):
                        if half == 0:
                            bank_free(u + c)
                        for k in range(half * HC1, (half + 1) * HC1):
                            last = nc.tensor.matmul(ps_work[(u + c) % WORK][:, 0, :], w2[:, k, c * P:(c + 1) * P],
                                                    h1T[:, k, :], start=(k == 0), stop=(k == C1 - 1))
                        if k == C1 - 1:
                            last.then_inc(work_made, 1)

            def layer3(t, _):
                u = work_no["layer3", t, None]
                bank_free(u)
                for k in range(C2):
                    made = work_no["layer2", t, None] + k
                    pe.wait_ge(work_out[made % 2], uses_of(made % 2, made + 1))
                    last = nc.tensor.matmul(ps_work[u % WORK][0:1, 0, :], small[:, w3_col + k:w3_col + k + 1],
                                            h2T[:, k, :], start=(k == 0), stop=(k == C2 - 1))
                last.then_inc(work_made, 1)

            def warm(_, n):
                for _ in range(n):
                    nc.tensor.matmul(ps_cols[0][:, 0, :], ident16[:], ident16[:], start=True, stop=True)

            pe.wait_ge(ident16_ready, 1)
            spread_ids(0)
            spread_ids(1)
            warm(None, 16)
            pe.wait_ge(small_in, 48)
            nc.tensor.transpose(ps_hot[0][:, 0, 0:NB_ROWS], small_rows[:, :],
                                ident[0:NB_ROWS, 0:NB_ROWS]).then_inc(small_turned, 1)
            pe.wait_ge(small_ready, 1)
            do = {"warm": warm, "one_hot": one_hot_products, "turn": turn, "products": products, "pick": pick,
                  "pairs": pairs, "layer1": layer1, "layer2": layer2, "layer3": layer3}
            for kind, t, what in ORDER:
                if kind != "split":
                    do[kind](t, what)

        def copies(eng, e, copy, relu, kind, t, what):
            if (kind, what) not in uses:
                return
            for b in range(uses[kind, what]):
                u = work_no[kind, t, what] + b
                if u % 2 != e:
                    continue
                eng.wait_ge(work_made, u + 1)
                bank = ps_work[u % WORK]
                if kind == "products":
                    made = bank[:].rearrange("p a b -> p (a b)")[:, 0:GPB * SG * (NF - 1)].rearrange(
                        "p (g s m) -> p g s m", s=SG, m=NF - 1)
                    for s in range(SG):
                        quad = slice(s * FP, min((s + 1) * FP, ROWS))
                        last = copy(gram[quad, 1:NF, b * GPB:(b + 1) * GPB].rearrange("p m g -> p g m"),
                                    made[quad, :, s, :])
                elif kind == "pick":
                    m0 = 1 + PICKS[what][b] * TPB
                    for m in range(m0, min(m0 + TPB, NF)):
                        quad = slice((m - m0) * NG, (m - m0 + 1) * NG)
                        last = copy(z[:, t % SLOTS, :, m * (m - 1) // 2:m * (m + 1) // 2],
                                    bank[quad, 0, :].rearrange("p (s n) -> p s n", s=SG)[:, :, 0:m])
                elif kind == "pairs":
                    chunks = CHUNKS[what][b]
                    nk = KZ[chunks[-1]][1]
                    last = copy(zT[0:nk, chunks[0]:chunks[-1] + 1, :], bank[0:nk, chunks[0]:chunks[-1] + 1, :])
                elif kind == "layer1":
                    for j in range(HC1):
                        c = b * HC1 + j
                        last = relu(h1T[:, c, :], layer1_bank(t, u)[:, j, :], small[:, c:c + 1])
                elif kind == "layer2":
                    last = relu(h2T[:, b, :], bank[:, 0, :], small[:, C1 + b:C1 + b + 1])
                else:
                    last = copy(y[:, t, :, :].rearrange("p g s -> p s g"),
                                bank[0:1, 0, :].rearrange("p (s g) -> p s g", s=SG))
                last.then_inc(work_out[e], 1)

        @block.vector
        def _(dve):
            def relu(o, i, bias):
                return nc.vector.tensor_scalar(o, i, bias, 0.0, ALU.add, ALU.max)

            dve.wait_ge(row_no_made, len(row_no))
            for n, r in enumerate(row_no):
                nc.vector.tensor_copy(row_no[r][:], row_no_int[:, n, 0:r]).then_inc(row_no_ready, 1)
            dve.wait_ge(row_no_ready, len(row_no))

            def split(i):
                dve.wait_ge(table_in[i], 32)
                nc.vector.tensor_tensor(left[i][:], table[i][:], upper_half(table[i][:]),
                                        ALU.subtract).then_inc(left_ready, 1)
                dve.wait_ge(left_ready, i + 1)
                nc.vector.tensor_tensor(low[i][:], left[i][:], upper_half(left[i][:]),
                                        ALU.subtract).then_inc(low_ready, 1)

            def match(n):
                r = RPP[hot_stage[n][1]]
                dve.wait_ge(hot_ids_ready, n + 1)
                if n >= 2:
                    dve.wait_ge(hot_made, n - 1)
                for j in range(r):
                    nc.vector.tensor_scalar(one_hot[:, n % 2, j, :], hot_ids[0:TP, n, :],
                                            row_no[r][0:TP, j:j + 1], None, ALU.is_equal).then_inc(hot_ready, 1)

            for kind, t, what in ORDER:
                if kind == "split":
                    split(what)
                    if what == 0:
                        match(0)
                if kind == "one_hot":
                    if hot_no[t, what] + 1 < len(hot_no):
                        match(hot_no[t, what] + 1)
                if (kind, t, what) == ("layer1", 0, 0):
                    dve.wait_ge(small_ready, 1)
                copies(dve, 0, nc.vector.tensor_copy, relu, kind, t, what)

        @block.scalar
        def _(act):
            def relu(o, i, bias):
                return nc.scalar.activation(o, i, ACT.Relu, bias=bias)

            def widen(n):
                pair, i = hot_stage[n]
                if n >= 2:
                    act.wait_ge(ids_turned, n - 1)
                f = ONE_HOT[i]
                one = idx[:, pair * PAIR:(pair + 1) * PAIR, f:f + 1]
                nc.scalar.copy(wide_ids[:, n % 2, :, :], one.to_broadcast([P, PAIR, P])).then_inc(wide_ready, 1)

            def take_ids(n):
                act.wait_ge(ids_turned, n + 1)
                nc.scalar.copy(hot_ids[:, n, :], ps_ids[:].rearrange("p b s -> p (b s)")).then_inc(hot_ids_ready, 1)

            act.wait_ge(ident_ready, 1)
            nc.scalar.copy(ident16[:], ident[:]).then_inc(ident16_ready, 1)
            act.wait_ge(ids_in, 16)
            widen(0)
            widen(1)
            take_ids(0)
            take_ids(1)
            widen(2)
            widen(3)
            act.wait_ge(small_turned, 1)
            nc.scalar.copy(small[:], ps_hot[0][:, 0, 0:NB_ROWS]).then_inc(small_ready, 1)
            act.wait_ge(small_ready, 1)
            for t in range(NT):
                nc.scalar.mul(cols[:, t, :, NF:FP], ident[:, 0:1].unsqueeze(2).to_broadcast([P, P, FP - NF]),
                              0.0).then_inc(pad_ready, 1)
            for kind, t, what in ORDER:
                if kind == "turn":
                    f0, step, n = RUNS[t // PAIR][what]
                    u = turn_no[t, what]
                    act.wait_ge(rows_turned, u + 1)
                    nc.scalar.copy(cols[:, t, :, f0:f0 + step * (n - 1) + 1:step].rearrange("p b f -> p f b"),
                                   ps_cols[u % 2][:, 0:n, :]).then_inc(cols_ready, 1)
                copies(act, 1, nc.scalar.copy, relu, kind, t, what)
                if kind == "one_hot":
                    n = hot_no[t, what]
                    if n + 2 < len(hot_no):
                        take_ids(n + 2)
                    if n + 4 < len(hot_no):
                        widen(n + 4)
                    act.wait_ge(hot_made, n + 1)
                    nc.scalar.copy(cols[:, t * PAIR:(t + 1) * PAIR, :, ONE_HOT[what]],
                                   ps_hot[n % 2][:]).then_inc(hot_cols, 1)



N_TABLES = 27
INPUTS = (["dense_ctx", "ids"] + [f"tbl_{i}" for i in range(N_TABLES)]
          + ["W_top1", "b_top1", "W_top2", "b_top2", "W_top3"])


def kernel(**inputs):
    import numpy as np
    import concourse.bacc as bacc
    from concourse.bass_utils import run_bass_kernel_spmd

    nc = bacc.Bacc("TRN2", target_bir_lowering=False, num_devices=1)
    arrays, args = {}, {}
    for name in INPUTS:
        a = np.ascontiguousarray(inputs[name])
        arrays[f"in_{name}"] = a
        args[name] = nc.dram_tensor(f"in_{name}", a.shape, mybir.dt.from_np(a.dtype), kind="ExternalInput").ap()
    out = nc.dram_tensor("out_y", (arrays["in_ids"].shape[0], 1), F32, kind="ExternalOutput").ap()
    build_tower(nc, args["dense_ctx"], args["ids"], [args[f"tbl_{i}"] for i in range(N_TABLES)],
                args["W_top1"], args["b_top1"], args["W_top2"], args["b_top2"], args["W_top3"], out)
    r = run_bass_kernel_spmd(nc, [arrays], core_ids=[0])
    return r.results[0]["out_y"]
```

```python
import concourse.bass as bass
from concourse import mybir
from contextlib import ExitStack

F32 = mybir.dt.float32
F16 = mybir.dt.float16
I32 = mybir.dt.int32
F32R = mybir.dt.float32r
U32 = mybir.dt.uint32
ALU = mybir.AluOpType
ACT = mybir.ActivationFunctionType


def arithmetic_runs(features, longest):
    runs, i = [], 0
    while i < len(features):
        n, step = 1, 1
        if i + 1 < len(features):
            step = features[i + 1] - features[i]
            while n < longest and i + n < len(features) and features[i + n] - features[i + n - 1] == step:
                n += 1
        runs.append((features[i], step, n))
        i += n
    return runs


def build_tower(nc, dense_ctx, ids, tables, W_top1, b_top1, W_top2, b_top2, W_top3, out):
    P = 128
    B, NF = ids.shape
    D = tables[0].shape[1]
    ND = dense_ctx.shape[1]
    NPAIR = NF * (NF - 1) // 2
    NZ, H1 = W_top1.shape
    H2 = W_top2.shape[1]
    NT = B // P
    PAIR = 2
    NPR = NT // PAIR
    SLOTS = PAIR
    FP = 32
    SG = P // FP
    NG = P // SG
    ROWS = (SG - 1) * FP + NF - 1
    TPB = 512 // P
    KZ = [(k, min(P, NZ - k)) for k in range(0, NZ, P)]
    LASTK = len(KZ) - 1
    C1, C2 = H1 // P, H2 // P
    HC1 = C1 // 2
    NB_ROWS = 2 * C2 + C1
    w3_col = C1 + C2
    assert D == P and B == NT * P and NT % PAIR == 0 and NZ == NPAIR + ND and NF <= FP
    assert HC1 == 2 and C2 == 2

    ONE_HOT = [14, 16, 18, 20, 22, 13, 8]
    HOTS = [6, 7]
    STAGED = 3
    TP = 125
    RPP = [tables[f].shape[0] // TP for f in ONE_HOT]
    assert all(tables[f].shape[0] == TP * r for f, r in zip(ONE_HOT, RPP))
    assert all(tables[f].shape[0] <= 2048 for f in ONE_HOT)
    MAXR = max(RPP)
    GATHERED = [[f for f in range(NF) if f not in ONE_HOT[:n]] for n in HOTS]
    PLACE = {f: i for i, f in enumerate(GATHERED[0])}
    RUNS = [arithmetic_runs(g, TPB) for g in GATHERED]
    assert set(GATHERED[1]) <= set(GATHERED[0])
    GPB = 512 // (SG * (NF - 1))
    NGB = NG // GPB

    PICKS = [[range(0, 2), range(2, 4)], [range(4, 6), range(6, -(-(NF - 1) // TPB))]]
    CHUNKS = [[range(0, 1)], [range(1, LASTK), range(LASTK, LASTK + 1)]]
    picked = (PICKS[0][-1][-1] + 1) * TPB
    assert NPAIR > KZ[0][1] and picked * (picked + 1) // 2 >= KZ[0][1]

    PARTS = 4
    PRODUCTS = [("products", part) for part in range(PARTS)]
    PRODUCTS_END = PRODUCTS[-1]
    CHAIN = PRODUCTS + [("pick", 0), ("pick", 1), ("pairs", 0), ("pairs", 1), ("layer1", 0), ("layer1", 1),
                        ("layer2", None), ("layer3", None)]

    def chain(t, between):
        stages = []
        for stage in CHAIN:
            stages += [(stage[0], t, stage[1])] + between.get(stage, [])
        return stages

    def turns(t, *runs):
        return [("turn", t, k) for k in runs]

    def split(*which):
        return [("split", None, i) for i in which]

    def spread(batch):
        return [("ids", None, batch)]

    def match(pair, i, *halves):
        return [("match", pair, (i, half)) for half in halves or (0, 1)]

    def hot(pair, i):
        return [("one_hot", pair, i)]

    def warm(n):
        return [("warm", None, n)]

    assert NPR == 2 and NT == 4
    LAST_RUNS = [range(4, len(r)) for r in RUNS]
    ORDER = spread(0) + split(0) + match(0, 0) + hot(0, 0) + match(0, 1) + spread(1) + split(1) + hot(0, 1)
    ORDER += match(0, 2) + split(2) + turns(0, 0) + hot(0, 2) + match(0, 3) + split(3) + turns(0, 1) + hot(0, 3)
    ORDER += match(0, 4) + split(4) + turns(0, 2) + hot(0, 4) + spread(2) + match(0, 5) + split(5) + turns(0, 3)
    ORDER += hot(0, 5) + match(1, 0) + turns(0, *LAST_RUNS[0]) + hot(1, 0)
    ORDER += chain(0, {
        PRODUCTS[0]: match(1, 1, 0),
        PRODUCTS[1]: match(1, 1, 1),
        PRODUCTS_END: turns(1, 0),
        ("pick", 0): turns(1, 1),
        ("pick", 1): hot(1, 1),
        ("pairs", 1): match(1, 2) + turns(1, 2),
        ("layer1", 1): spread(3) + hot(1, 2),
        ("layer2", None): split(6) + match(1, 3, 0) + turns(1, 3)})
    ORDER += match(1, 3, 1) + turns(1, *LAST_RUNS[0]) + hot(1, 3)
    ORDER += chain(1, {
        PRODUCTS[0]: match(1, 4, 0),
        PRODUCTS[1]: match(1, 4, 1),
        PRODUCTS_END: turns(2, 0),
        ("pick", 0): turns(2, 1),
        ("pick", 1): hot(1, 4),
        ("pairs", 1): match(1, 5) + turns(2, 2),
        ("layer1", 1): hot(1, 5),
        ("layer2", None): match(1, 6) + turns(2, 3) + hot(1, 6) + turns(2, *LAST_RUNS[1])})
    ORDER += chain(2, {
        PRODUCTS_END: turns(3, 0),
        ("pick", 0): turns(3, 1),
        ("pick", 1): turns(3, 2),
        ("layer2", None): turns(3, 3, *LAST_RUNS[1])})
    ORDER += chain(3, {
        PRODUCTS_END: warm(12),
        ("pick", 1): warm(6),
        ("pairs", 0): warm(4),
        ("pairs", 1): warm(2)})
    counted = [stage for stage in ORDER if stage[0] not in ("ids", "match", "warm")]
    assert len(set(counted)) == len(counted)
    assert len(counted) == sum(PAIR * (len(r) + len(CHAIN)) for r in RUNS) + sum(HOTS) + len(ONE_HOT)

    WORK = 3
    uses = {**{stage: NGB // PARTS for stage in PRODUCTS},
            ("pick", 0): len(PICKS[0]), ("pick", 1): len(PICKS[1]), ("pairs", 0): len(CHUNKS[0]),
            ("pairs", 1): len(CHUNKS[1]), ("layer1", 0): 0, ("layer1", 1): C1 // HC1, ("layer2", None): C2,
            ("layer3", None): 1}
    turn_no, hot_no, work_no = {}, {}, {}
    n_work = 0
    for kind, t, what in ORDER:
        if kind == "turn":
            turn_no[t, what] = len(turn_no)
        elif kind == "one_hot":
            hot_no[t, what] = len(hot_no)
        elif kind not in ("split", "match", "ids", "warm"):
            work_no[kind, t, what] = n_work
            n_work += uses[kind, what]
    hot_stage = {n: stage for stage, n in hot_no.items()}
    matches = [(hot_no[t, what[0]], what[1]) for kind, t, what in ORDER if kind == "match"]
    assert matches == [(n, half) for n in range(len(hot_no)) for half in range(2)]
    BATCH = 4
    IDS = [range(0, 2)] + [range(n, min(n + BATCH, len(hot_no))) for n in range(2, len(hot_no), BATCH)]
    ids_batch = {n: b for b, batch in enumerate(IDS) for n in batch}
    assert [what for kind, _, what in ORDER if kind == "ids"] == list(range(len(IDS)))
    assert all(ORDER.index(("split", None, i)) < ORDER.index(("one_hot", pair, i)) for pair, i in hot_no)

    def work_end(kind, t, what=None):
        return work_no[kind, t, what] + uses[kind, what]

    def uses_of(e, n):
        return (n + 1 - e) // 2

    def hots_before(n):
        return sum(RPP[hot_stage[m][1]] for m in range(n))

    with ExitStack() as ctx:
        def sb(name, shape, dt=F32):
            return ctx.enter_context(nc.sbuf_tensor(name, shape, dt))

        def psum(name, shape, dt=F32):
            return ctx.enter_context(nc.psum_tensor(name, shape, dt))

        def layer1_bank(t, u):
            return ps_hot[u % 2] if t == NT - 1 else ps_work[u % WORK]

        def sem(name):
            return ctx.enter_context(nc.semaphore(name))

        idx = sb("idx", [P, NT, NF], I32)
        rows = sb("rows", [P, SLOTS, len(PLACE), D])
        cols = sb("cols", [P, NT, P, FP])
        gram = sb("gram", [ROWS, NF, NG])
        z = sb("z", [NG, SLOTS, SG, NZ])
        zT = sb("zT", [P, len(KZ), P])
        h1T = sb("h1T", [P, C1, P])
        h2T = sb("h2T", [P, C2, P])
        y = sb("y", [1, NT, NG, SG])
        w1 = sb("w1", [P, len(KZ), H1])
        w2 = sb("w2", [P, C1, H2])
        small_rows = sb("small_rows", [NB_ROWS, P])
        small = sb("small", [P, NB_ROWS])
        ident = sb("ident", [P, P])
        table = sb("table", [TP, STAGED, MAXR, D])
        high = [sb(f"high{i}", [TP, RPP[i], D], F32R) for i in range(len(ONE_HOT))]
        left = [sb(f"left{i}", [TP, RPP[i], D], F32R) for i in range(len(ONE_HOT))]
        row_no_int = sb("row_no_int", [P, 2, MAXR], I32)
        row_no = {r: sb(f"row_no{r}", [P, r]) for r in sorted(set(RPP))}
        ids16 = sb("ids16", [P, NT, NF], F16)
        hot_ids = sb("hot_ids", [P, 2, BATCH, PAIR * P], F16)
        one_hot = sb("one_hot", [TP, 2, MAXR, PAIR * P], F32R)
        ident16 = sb("ident16", [P, P], F16)

        ps_cols = [psum(f"ps_cols{i}", [P, TPB, P]) for i in range(2)]
        ps_work = [psum(f"ps_work{i}", [P, TPB, P]) for i in range(WORK)]
        ps_ids = psum("ps_ids", [P, BATCH, PAIR, P], F16)
        ps_hot = [psum(f"ps_hot{i}", [P, PAIR, P]) for i in range(2)]

        ids_in = sem("ids_in")
        w1_in = sem("w1_in")
        w2_in = sem("w2_in")
        small_in = sem("small_in")
        table_in = [sem(f"table_in{i}") for i in range(len(ONE_HOT))]
        dense_in = [sem(f"dense_in{s}") for s in range(SLOTS)]
        ident_zero = sem("ident_zero")
        ident_ready = sem("ident_ready")
        ident16_ready = sem("ident16_ready")
        high_ready = sem("high_ready")
        left_ready = sem("left_ready")
        row_no_made = sem("row_no_made")
        row_no_ready = sem("row_no_ready")
        pad_ready = sem("pad_ready")
        rows_in = [[sem(f"rows_in{s}_{k}") for k in range(max(map(len, RUNS)))] for s in range(SLOTS)]
        small_turned = sem("small_turned")
        small_ready = sem("small_ready")
        ids16_ready = sem("ids16_ready")
        ids_turned = sem("ids_turned")
        hot_ids_ready = sem("hot_ids_ready")
        hot_ready = sem("hot_ready")
        hot_made = sem("hot_made")
        hot_cols = sem("hot_cols")
        rows_turned = sem("rows_turned")
        cols_ready = sem("cols_ready")
        work_made = sem("work_made")
        work_out = [sem("work_out_dve"), sem("work_out_act")]
        out_done = sem("out_done")

        block = ctx.enter_context(nc.Block())

        @block.sync
        def _(sp):
            sp.dma_start(idx[:], ids.rearrange("(t p) f -> p t f", p=P)).then_inc(ids_in, 16)
            wide = TP // 16 * 16

            def load_table(i):
                if i >= STAGED:
                    sp.wait_ge(left_ready, i - STAGED + 1)
                whole = tables[ONE_HOT[i]].rearrange("(p r) d -> p r d", p=TP)
                slot = table[:, i % STAGED, 0:RPP[i], :]
                sp.dma_start(slot[0:wide], whole[0:wide]).then_inc(table_in[i], 16)
                sp.dma_start(slot[wide:TP], whole[wide:TP]).then_inc(table_in[i], 16)

            def load_dense(t):
                if t >= SLOTS:
                    sp.wait_ge(work_made, work_end("pairs", t - SLOTS, 1))
                sp.dma_start(z[:, t % SLOTS, :, NPAIR:NZ], dense[t]).then_inc(dense_in[t % SLOTS], 16)

            dense = dense_ctx.rearrange("(t g s) d -> t g s d", t=NT, s=SG)
            load_table(0)
            sp.dma_start(small_rows[0:C1, :], b_top1.rearrange("(c p) -> c p", p=P)).then_inc(small_in, 16)
            sp.dma_start(small_rows[C1:C1 + C2, :], b_top2.rearrange("(c p) -> c p", p=P)).then_inc(small_in, 16)
            sp.dma_start(small_rows[w3_col:w3_col + C2, :],
                         W_top3.rearrange("(c p) one -> c (p one)", p=P)).then_inc(small_in, 16)
            for i in range(1, STAGED):
                load_table(i)
            nfull = NZ // P
            sp.dma_start(w1[:, 0:nfull, :],
                         W_top1[0:nfull * P, :].rearrange("(k p) o -> p k o", p=P)).then_inc(w1_in, 16)
            sp.dma_start(w1[0:NZ - nfull * P, nfull, :], W_top1[nfull * P:NZ, :]).then_inc(w1_in, 16)
            sp.dma_start(w2[:], W_top2.rearrange("(k p) o -> p k o", p=P)).then_inc(w2_in, 16)
            for t in range(SLOTS):
                load_dense(t)
            for i in range(STAGED, len(ONE_HOT)):
                load_table(i)
            for t in range(SLOTS, NT):
                load_dense(t)
            for e in range(2):
                sp.wait_ge(work_out[e], uses_of(e, n_work))
            sp.dma_start(out.rearrange("b one -> one b"),
                         y[:].rearrange("p t g s -> p (t g s)")).then_inc(out_done, 16)
            sp.wait_ge(out_done, 16)

        @block.gpsimd
        def _(pool):
            nc.gpsimd.memset(ident[:], 0.0).then_inc(ident_zero, 1)
            for n, r in enumerate(row_no):
                nc.gpsimd.iota(row_no_int[:, n, 0:r], pattern=[[1, r]], base=0,
                               channel_multiplier=r).then_inc(row_no_made, 1)
            pool.wait_ge(ident_zero, 1)
            nc.gpsimd.affine_select(out=ident[:], in_=ident[:], compare_op=ALU.not_equal, fill=1.0, base=0,
                                    pattern=[[-1, P]], channel_multiplier=1).then_inc(ident_ready, 1)
            pool.wait_ge(ids_in, 16)
            for t in range(NT):
                for k, (f0, step, n) in enumerate(RUNS[t // PAIR]):
                    if t >= SLOTS:
                        last_f = f0 + step * (n - 1)
                        there = [j for j, r in enumerate(RUNS[t // PAIR - 1]) if r[0] <= last_f][-1]
                        pool.wait_ge(rows_turned, turn_no[t - SLOTS, there] + 1)
                    for f in range(f0, f0 + step * n, step):
                        nc.gpsimd.indirect_dma_start(
                            out=rows[:, t % SLOTS, PLACE[f], :], out_offset=None, in_=tables[f],
                            in_offset=bass.IndirectOffsetOnAxis(ap=idx[:, t, f:f + 1].bitcast(U32), axis=0),
                        ).then_inc(rows_in[t % SLOTS][k], 16)

        @block.tensor
        def _(pe):
            def bank_free(u):
                if u >= WORK:
                    pe.wait_ge(work_out[(u - WORK) % 2], uses_of((u - WORK) % 2, u - WORK + 1))

            def copied_out(kind, t, what=None):
                for e in range(2):
                    pe.wait_ge(work_out[e], uses_of(e, work_end(kind, t, what)))

            def spread_ids(_, b):
                if b == 0:
                    pe.wait_ge(ids16_ready, 1)
                else:
                    pe.wait_ge(hot_ids_ready, b)
                for i, n in enumerate(IDS[b]):
                    pair, which = hot_stage[n]
                    f = ONE_HOT[which]
                    for p in range(PAIR):
                        last = nc.tensor.transpose(ps_ids[:, i, p, :],
                                                   ids16[:, pair * PAIR + p, f:f + 1].to_broadcast([P, P]), ident16[:])
                last.then_inc(ids_turned, 1)

            def one_hot_products(pair, i):
                n = hot_no[pair, i]
                if n >= 2:
                    pe.wait_ge(hot_cols, n - 1)
                pe.wait_ge(left_ready, i + 1)
                parts = [high[i], left[i]]
                for j in range(RPP[i]):
                    pe.wait_ge(hot_ready, hots_before(n) + j + 1)
                    for q, part in enumerate(parts):
                        last = nc.tensor.matmul(ps_hot[n % 2][:].rearrange("p b s -> p (b s)"),
                                                part[:, j, :], one_hot[:, n % 2, j, :],
                                                start=(j == 0 and q == 0),
                                                stop=(j == RPP[i] - 1 and q == len(parts) - 1))
                last.then_inc(hot_made, 1)

            def turn(t, k):
                f0, step, n = RUNS[t // PAIR][k]
                u = turn_no[t, k]
                before = sum(RUNS[q][k][2] for q in range(t // SLOTS))
                pe.wait_ge(rows_in[t % SLOTS][k], 16 * (before + n))
                if u >= 2:
                    pe.wait_ge(cols_ready, u - 1)
                for j in range(n):
                    last = nc.tensor.transpose(ps_cols[u % 2][:, j, :], rows[:, t % SLOTS, PLACE[f0 + step * j], :], ident[:])
                last.then_inc(rows_turned, 1)

            def products(t, part):
                if t == 0:
                    pe.wait_ge(pad_ready, NT)
                pe.wait_ge(cols_ready, turn_no[t, len(RUNS[t // PAIR]) - 1] + 1)
                pe.wait_ge(hot_cols, max(n for (pair, _), n in hot_no.items() if pair == t // PAIR) + 1)
                width = SG * (NF - 1)
                for gb in range(part * NGB // PARTS, (part + 1) * NGB // PARTS):
                    u = work_no["products", t, 0] + gb
                    bank_free(u)
                    flat = ps_work[u % WORK][:].rearrange("p a b -> p (a b)")
                    for j in range(GPB):
                        s0 = (gb * GPB + j) * SG
                        group = cols[:, t, s0:s0 + SG, :]
                        last = nc.tensor.matmul(
                            flat[0:ROWS, j * width:(j + 1) * width].rearrange("p (s m) -> p s m", s=SG),
                            group.rearrange("p s f -> p (s f)")[:, 0:ROWS], group[:, :, 1:NF], start=True, stop=True)
                    last.then_inc(work_made, 1)

            def pick(t, half):
                if half == 0:
                    copied_out("products", t, PARTS - 1)
                for b, picks in enumerate(PICKS[half]):
                    u = work_no["pick", t, half] + b
                    bank_free(u)
                    for i, q in enumerate(picks):
                        m = 1 + q * TPB
                        n = min(TPB, NF - m)
                        last = nc.tensor.transpose(ps_work[u % WORK][0:n * NG, i, 0:ROWS],
                                                   gram[0:ROWS, m:m + n, :].rearrange("p m g -> p (m g)"),
                                                   ident[0:ROWS, 0:ROWS])
                    last.then_inc(work_made, 1)

            def pairs(t, half):
                copied_out("pick", t, half)
                for b, chunks in enumerate(CHUNKS[half]):
                    u = work_no["pairs", t, half] + b
                    bank_free(u)
                    if chunks[-1] == LASTK:
                        pe.wait_ge(dense_in[t % SLOTS], 16 * (t // SLOTS + 1))
                    for k in chunks:
                        k0, nk = KZ[k]
                        for s in range(SG):
                            last = nc.tensor.transpose(ps_work[u % WORK][0:nk, k, s * NG:(s + 1) * NG],
                                                       z[:, t % SLOTS, s, k0:k0 + nk], ident[0:NG, 0:NG])
                    last.then_inc(work_made, 1)

            def layer1(t, half):
                copied_out("pairs", t, half)
                if t == 0 and half == 0:
                    pe.wait_ge(w1_in, 32)
                for c in range(C1):
                    u = work_no["layer1", t, 1] + c // HC1
                    if half == 0 and c % HC1 == 0 and t < NT - 1:
                        bank_free(u)
                    for k in [k for chunks in CHUNKS[half] for k in chunks]:
                        nk = KZ[k][1]
                        last = nc.tensor.matmul(layer1_bank(t, u)[:, c % HC1, :], w1[0:nk, k, c * P:(c + 1) * P],
                                                zT[0:nk, k, :], start=(k == 0 and c % HC1 == 0), stop=(k == LASTK),
                                                skip_group_check=True)
                    if half == 1 and c % HC1 == HC1 - 1:
                        last.then_inc(work_made, 1)

            def layer2(t, _):
                if t == 0:
                    pe.wait_ge(w2_in, 16)
                u = work_no["layer2", t, None]
                for half in range(C1 // HC1):
                    made = work_no["layer1", t, 1] + half
                    pe.wait_ge(work_out[made % 2], uses_of(made % 2, made + 1))
                    for c in range(C2):
                        if half == 0:
                            bank_free(u + c)
                        for k in range(half * HC1, (half + 1) * HC1):
                            last = nc.tensor.matmul(ps_work[(u + c) % WORK][:, 0, :], w2[:, k, c * P:(c + 1) * P],
                                                    h1T[:, k, :], start=(k == 0), stop=(k == C1 - 1))
                        if k == C1 - 1:
                            last.then_inc(work_made, 1)

            def layer3(t, _):
                u = work_no["layer3", t, None]
                bank_free(u)
                for k in range(C2):
                    made = work_no["layer2", t, None] + k
                    pe.wait_ge(work_out[made % 2], uses_of(made % 2, made + 1))
                    last = nc.tensor.matmul(ps_work[u % WORK][0:1, 0, :], small[:, w3_col + k:w3_col + k + 1],
                                            h2T[:, k, :], start=(k == 0), stop=(k == C2 - 1))
                last.then_inc(work_made, 1)

            def warm(_, n):
                for _ in range(n):
                    nc.tensor.matmul(ps_cols[0][:, 0, :], ident16[:], ident16[:], start=True, stop=True)

            pe.wait_ge(ident16_ready, 1)
            spread_ids(None, 0)
            warm(None, 16)
            pe.wait_ge(small_in, 48)
            nc.tensor.transpose(ps_hot[0][:, 0, 0:NB_ROWS], small_rows[:, :],
                                ident[0:NB_ROWS, 0:NB_ROWS]).then_inc(small_turned, 1)
            pe.wait_ge(small_ready, 1)
            do = {"warm": warm, "ids": spread_ids, "one_hot": one_hot_products, "turn": turn,
                  "products": products, "pick": pick, "pairs": pairs, "layer1": layer1, "layer2": layer2,
                  "layer3": layer3}
            for kind, t, what in ORDER:
                if kind not in ("split", "match") and (kind, what) != ("ids", 0):
                    do[kind](t, what)

        def copies(eng, e, copy, relu, kind, t, what):
            if (kind, what) not in uses:
                return
            for b in range(uses[kind, what]):
                u = work_no[kind, t, what] + b
                if u % 2 != e:
                    continue
                eng.wait_ge(work_made, u + 1)
                bank = ps_work[u % WORK]
                if kind == "products":
                    gb = what * NGB // PARTS + b
                    made = bank[:].rearrange("p a b -> p (a b)")[:, 0:GPB * SG * (NF - 1)].rearrange(
                        "p (g s m) -> p g s m", s=SG, m=NF - 1)
                    for s in range(SG):
                        quad = slice(s * FP, min((s + 1) * FP, ROWS))
                        last = copy(gram[quad, 1:NF, gb * GPB:(gb + 1) * GPB].rearrange("p m g -> p g m"),
                                    made[quad, :, s, :])
                elif kind == "pick":
                    for i, q in enumerate(PICKS[what][b]):
                        m0 = 1 + q * TPB
                        for m in range(m0, min(m0 + TPB, NF)):
                            quad = slice((m - m0) * NG, (m - m0 + 1) * NG)
                            last = copy(z[:, t % SLOTS, :, m * (m - 1) // 2:m * (m + 1) // 2],
                                        bank[quad, i, :].rearrange("p (s n) -> p s n", s=SG)[:, :, 0:m])
                elif kind == "pairs":
                    chunks = CHUNKS[what][b]
                    nk = KZ[chunks[-1]][1]
                    last = copy(zT[0:nk, chunks[0]:chunks[-1] + 1, :], bank[0:nk, chunks[0]:chunks[-1] + 1, :])
                elif kind == "layer1":
                    for j in range(HC1):
                        c = b * HC1 + j
                        last = relu(h1T[:, c, :], layer1_bank(t, u)[:, j, :], small[:, c:c + 1])
                elif kind == "layer2":
                    last = relu(h2T[:, b, :], bank[:, 0, :], small[:, C1 + b:C1 + b + 1])
                else:
                    last = copy(y[:, t, :, :].rearrange("p g s -> p s g"),
                                bank[0:1, 0, :].rearrange("p (s g) -> p s g", s=SG))
                last.then_inc(work_out[e], 1)

        @block.vector
        def _(dve):
            def relu(o, i, bias):
                return nc.vector.tensor_scalar(o, i, bias, 0.0, ALU.add, ALU.max)

            dve.wait_ge(row_no_made, len(row_no))
            for n, r in enumerate(row_no):
                nc.vector.tensor_copy(row_no[r][:], row_no_int[:, n, 0:r]).then_inc(row_no_ready, 1)
            dve.wait_ge(row_no_ready, len(row_no))

            def split(i):
                dve.wait_ge(table_in[i], 32)
                dve.wait_ge(high_ready, i + 1)
                nc.vector.tensor_tensor(left[i][:], table[:, i % STAGED, 0:RPP[i], :], high[i][:].bitcast(F32),
                                        ALU.subtract).then_inc(left_ready, 1)

            def match(n, half):
                r = RPP[hot_stage[n][1]]
                b = ids_batch[n]
                dve.wait_ge(hot_ids_ready, b + 1)
                if n >= 2:
                    dve.wait_ge(hot_made, n - 1)
                for j in (range(r // 2) if half == 0 else range(r // 2, r)):
                    nc.vector.tensor_scalar(one_hot[:, n % 2, j, :], hot_ids[0:TP, b % 2, n - IDS[b][0], :],
                                            row_no[r][0:TP, j:j + 1], None, ALU.is_equal).then_inc(hot_ready, 1)

            for kind, t, what in ORDER:
                if kind == "split":
                    split(what)
                if kind == "match":
                    match(hot_no[t, what[0]], what[1])
                if (kind, t, what) == ("layer1", 0, 0):
                    dve.wait_ge(small_ready, 1)
                copies(dve, 0, nc.vector.tensor_copy, relu, kind, t, what)

        @block.scalar
        def _(act):
            def relu(o, i, bias):
                return nc.scalar.activation(o, i, ACT.Relu, bias=bias)

            def round_high(i):
                act.wait_ge(table_in[i], 32)
                nc.scalar.copy(high[i][:], table[:, i % STAGED, 0:RPP[i], :]).then_inc(high_ready, 1)

            def take_ids(b):
                act.wait_ge(ids_turned, b + 1)
                ns = IDS[b]
                if b >= 2:
                    act.wait_ge(hot_ready, hots_before(IDS[b - 2][-1] + 1))
                nc.scalar.copy(hot_ids[:, b % 2, 0:len(ns), :],
                               ps_ids[:, 0:len(ns), :, :].rearrange("p i b s -> p i (b s)")).then_inc(hot_ids_ready, 1)

            def pad(t):
                nc.scalar.mul(cols[:, t, :, NF:FP], ident[:, 0:1].unsqueeze(2).to_broadcast([P, P, FP - NF]),
                              0.0).then_inc(pad_ready, 1)

            act.wait_ge(ident_ready, 1)
            nc.scalar.copy(ident16[:], ident[:]).then_inc(ident16_ready, 1)
            act.wait_ge(ids_in, 16)
            nc.scalar.copy(ids16[:], idx[:]).then_inc(ids16_ready, 1)
            take_ids(0)
            round_high(0)
            act.wait_ge(small_turned, 1)
            nc.scalar.copy(small[:], ps_hot[0][:, 0, 0:NB_ROWS]).then_inc(small_ready, 1)
            for kind, t, what in ORDER:
                if kind == "split" and what + 1 < len(ONE_HOT):
                    round_high(what + 1)
                if kind == "ids" and what > 0:
                    take_ids(what)
                if kind == "turn":
                    f0, step, n = RUNS[t // PAIR][what]
                    u = turn_no[t, what]
                    act.wait_ge(rows_turned, u + 1)
                    nc.scalar.copy(cols[:, t, :, f0:f0 + step * (n - 1) + 1:step].rearrange("p b f -> p f b"),
                                   ps_cols[u % 2][:, 0:n, :]).then_inc(cols_ready, 1)
                    if t == 0 and what < NT:
                        pad(what)
                copies(act, 1, nc.scalar.copy, relu, kind, t, what)
                if kind == "one_hot":
                    n = hot_no[t, what]
                    act.wait_ge(hot_made, n + 1)
                    nc.scalar.copy(cols[:, t * PAIR:(t + 1) * PAIR, :, ONE_HOT[what]],
                                   ps_hot[n % 2][:]).then_inc(hot_cols, 1)


N_TABLES = 27
INPUTS = (["dense_ctx", "ids"] + [f"tbl_{i}" for i in range(N_TABLES)]
          + ["W_top1", "b_top1", "W_top2", "b_top2", "W_top3"])


def kernel(**inputs):
    import numpy as np
    import concourse.bacc as bacc
    from concourse.bass_utils import run_bass_kernel_spmd

    nc = bacc.Bacc("TRN2", target_bir_lowering=False, num_devices=1)
    arrays, args = {}, {}
    for name in INPUTS:
        a = np.ascontiguousarray(inputs[name])
        arrays[f"in_{name}"] = a
        args[name] = nc.dram_tensor(f"in_{name}", a.shape, mybir.dt.from_np(a.dtype), kind="ExternalInput").ap()
    out = nc.dram_tensor("out_y", (arrays["in_ids"].shape[0], 1), F32, kind="ExternalOutput").ap()
    build_tower(nc, args["dense_ctx"], args["ids"], [args[f"tbl_{i}"] for i in range(N_TABLES)],
                args["W_top1"], args["b_top1"], args["W_top2"], args["b_top2"], args["W_top3"], out)
    r = run_bass_kernel_spmd(nc, [arrays], core_ids=[0])
    return r.results[0]["out_y"]
```
